# Optimizing a Trainium2 kernel written in Bass

```python
import numpy as np
import jax
import jax.numpy as jnp

def _softmax(x, axis=-1):
    return jax.nn.softmax(x, axis=axis)

def _gelu(x):
    return jax.nn.gelu(x, approximate=True)

def _silu(x):
    return jax.nn.silu(x)

def _sigmoid(x):
    return jax.nn.sigmoid(x)

def _layernorm(x, axis=-1, eps=1e-05):
    m = jnp.mean(x, axis=axis, keepdims=True)
    v = jnp.var(x, axis=axis, keepdims=True)
    return (x - m) / jnp.sqrt(v + eps)

def _scatter_add(tgt, idx, src, axis=0):
    return tgt.at[idx].add(src)

def _segment_sum(src, seg, n):
    return jax.ops.segment_sum(src, seg, n)
kernel_name = 'mk_gnn_resnorm_d2_gnn_r8_99bf25'

def setup_inputs(seed: int=0):
    np.random.seed(seed)
    _w = jnp.asarray

    def _rec_inputs():
        import jax
        import jax.numpy as jnp
        _gk = jax.random.key(seed)
        x = -8.776e-05 + 1 * jax.random.normal(jax.random.fold_in(_gk, 1), (1250, 512), jnp.float32)
        src = jax.random.randint(jax.random.fold_in(_gk, 2), (40000,), 0, 1250, jnp.int32)
        dst = jnp.minimum((1250 * jax.random.uniform(jax.random.fold_in(_gk, 3), (40000,)) ** 2.0).astype(jnp.int32), 9999)
        _o = jnp.argsort(dst, stable=True)
        src = src[_o]
        dst = dst[_o]
        return (x, src, dst)
    x, src, dst = _rec_inputs()

    def _L0_gnn_setup():
        import jax, jax.numpy as jnp
        import numpy as np
        N_EMBD = 512
        HEADS = 8
        C = N_EMBD // HEADS
        N_NODES = 1250
        N_EDGES = 20000
        NEG_SLOPE = 0.2
        LN_EPS = 1e-05

        def _layer_norm(x, g, b):
            mu = jnp.mean(x, axis=-1, keepdims=True)
            var = jnp.mean(jnp.square(x - mu), axis=-1, keepdims=True)
            return (x - mu) * jax.lax.rsqrt(var + LN_EPS) * g + b

        def _gatv2(x, edge_index, Wl, Wr, att, gat_bias):
            src, dst = (edge_index[0], edge_index[1])
            xl = (x @ Wl).reshape(-1, HEADS, C)
            xr = (x @ Wr).reshape(-1, HEADS, C)
            h = jax.nn.leaky_relu(xl[src] + xr[dst], NEG_SLOPE)
            e = jnp.einsum('ehc,hc->eh', h, att)
            m = jax.ops.segment_max(e, dst, num_segments=N_NODES)
            ex = jnp.exp(e - m[dst])
            denom = jax.ops.segment_sum(ex, dst, num_segments=N_NODES)
            alpha = ex / (denom[dst] + 1e-16)
            msg = alpha[..., None] * xl[src]
            out = jax.ops.segment_sum(msg, dst, num_segments=N_NODES)
            return out.reshape(-1, HEADS * C) + gat_bias
        key = jax.random.key(seed)
        ks = jax.random.split(key, 12)
        s = 0.02
        x = jax.random.normal(ks[0], (N_NODES, N_EMBD), dtype=jnp.float32)
        edge_index = jax.random.randint(ks[1], (2, N_EDGES), 0, N_NODES, dtype=jnp.int32)
        return {'x': x, 'edge_index': edge_index, 'ln1_g': jnp.ones((N_EMBD,), jnp.float32), 'ln1_b': jnp.zeros((N_EMBD,), jnp.float32), 'Wl': jax.random.normal(ks[2], (N_EMBD, HEADS * C), jnp.float32) * s, 'Wr': jax.random.normal(ks[3], (N_EMBD, HEADS * C), jnp.float32) * s, 'att': jax.random.normal(ks[4], (HEADS, C), jnp.float32) * s, 'gat_bias': jnp.zeros((HEADS * C,), jnp.float32), 'ln2_g': jnp.ones((N_EMBD,), jnp.float32), 'ln2_b': jnp.zeros((N_EMBD,), jnp.float32), 'W1': jax.random.normal(ks[5], (N_EMBD, 4 * N_EMBD), jnp.float32) * s, 'b1': jnp.zeros((4 * N_EMBD,), jnp.float32), 'W2': jax.random.normal(ks[6], (4 * N_EMBD, N_EMBD), jnp.float32) * s, 'b2': jnp.zeros((N_EMBD,), jnp.float32)}
    _L0_gnn_all = _L0_gnn_setup()
    _L0_gnn_in = {k: v for k, v in _L0_gnn_all.items() if k in ('ln1_g', 'ln1_b', 'Wl', 'Wr', 'att', 'gat_bias', 'ln2_g', 'ln2_b', 'W1', 'b1', 'W2', 'b2')}
    del _L0_gnn_all

    def _L1_gnn_setup():
        import jax, jax.numpy as jnp
        import numpy as np
        N = 1250
        E = 20000
        D = 512
        EPS = 1e-05

        def _lin_params(key, out_d, in_d, bias=True):
            k1, k2 = jax.random.split(key)
            s = 1.0 / np.sqrt(in_d)
            W = jax.random.uniform(k1, (out_d, in_d), jnp.float32, -s, s)
            if bias:
                b = jax.random.uniform(k2, (out_d,), jnp.float32, -s, s)
                return (W, b)
            return (W,)

        def _sage_conv(x, src, dst, Wp, bp, Wl, bl, Wr):
            h = jax.nn.relu(x @ Wp.T + bp)
            agg = jax.ops.segment_sum(h[src], dst, num_segments=N)
            cnt = jax.ops.segment_sum(jnp.ones((src.shape[0],), x.dtype), dst, num_segments=N)
            agg = agg / jnp.maximum(cnt, 1.0)[:, None]
            return agg @ Wl.T + bl + x @ Wr.T

        def _relu_ln(x, g, b):
            x = jax.nn.relu(x)
            mu = jnp.mean(x, axis=-1, keepdims=True)
            var = jnp.mean(jnp.square(x - mu), axis=-1, keepdims=True)
            return (x - mu) * jax.lax.rsqrt(var + EPS) * g + b
        key = jax.random.key(seed)
        ks = jax.random.split(key, 16)
        inp = {'x': jax.random.normal(ks[0], (N, D), jnp.float32), 'edge_index': jax.random.randint(ks[1], (2, E), 0, N, jnp.int64)}
        ki = 2
        for l in range(3):
            Wp, bp = _lin_params(ks[ki], D, D)
            ki += 1
            Wl, bl = _lin_params(ks[ki], D, D)
            ki += 1
            Wr, = _lin_params(ks[ki], D, D, bias=False)
            ki += 1
            inp[f'Wp{l}'] = Wp
            inp[f'bp{l}'] = bp
            inp[f'Wl{l}'] = Wl
            inp[f'bl{l}'] = bl
            inp[f'Wr{l}'] = Wr
            if l < 2:
                inp[f'g{l}'] = jnp.ones((D,), jnp.float32)
                inp[f'be{l}'] = jnp.zeros((D,), jnp.float32)
        return inp
    _L1_gnn_all = _L1_gnn_setup()
    _L1_gnn_in = {k: v for k, v in _L1_gnn_all.items() if k in ('Wp0', 'bp0', 'Wl0', 'bl0', 'Wr0', 'g0', 'be0', 'Wp1', 'bp1', 'Wl1', 'bl1', 'Wr1', 'g1', 'be1', 'Wp2', 'bp2', 'Wl2', 'bl2', 'Wr2')}
    del _L1_gnn_all
    return {'x': x, 'src': src, 'dst': dst, 'L0_gnn_ln1_g': _L0_gnn_in['ln1_g'], 'L0_gnn_ln1_b': _L0_gnn_in['ln1_b'], 'L0_gnn_Wl': _L0_gnn_in['Wl'], 'L0_gnn_Wr': _L0_gnn_in['Wr'], 'L0_gnn_att': _L0_gnn_in['att'], 'L0_gnn_gat_bias': _L0_gnn_in['gat_bias'], 'L0_gnn_ln2_g': _L0_gnn_in['ln2_g'], 'L0_gnn_ln2_b': _L0_gnn_in['ln2_b'], 'L0_gnn_W1': _L0_gnn_in['W1'], 'L0_gnn_b1': _L0_gnn_in['b1'], 'L0_gnn_W2': _L0_gnn_in['W2'], 'L0_gnn_b2': _L0_gnn_in['b2'], 'L1_gnn_Wp0': _L1_gnn_in['Wp0'], 'L1_gnn_bp0': _L1_gnn_in['bp0'], 'L1_gnn_Wl0': _L1_gnn_in['Wl0'], 'L1_gnn_bl0': _L1_gnn_in['bl0'], 'L1_gnn_Wr0': _L1_gnn_in['Wr0'], 'L1_gnn_g0': _L1_gnn_in['g0'], 'L1_gnn_be0': _L1_gnn_in['be0'], 'L1_gnn_Wp1': _L1_gnn_in['Wp1'], 'L1_gnn_bp1': _L1_gnn_in['bp1'], 'L1_gnn_Wl1': _L1_gnn_in['Wl1'], 'L1_gnn_bl1': _L1_gnn_in['bl1'], 'L1_gnn_Wr1': _L1_gnn_in['Wr1'], 'L1_gnn_g1': _L1_gnn_in['g1'], 'L1_gnn_be1': _L1_gnn_in['be1'], 'L1_gnn_Wp2': _L1_gnn_in['Wp2'], 'L1_gnn_bp2': _L1_gnn_in['bp2'], 'L1_gnn_Wl2': _L1_gnn_in['Wl2'], 'L1_gnn_bl2': _L1_gnn_in['bl2'], 'L1_gnn_Wr2': _L1_gnn_in['Wr2']}

def reference(x, src, dst, L0_gnn_ln1_g, L0_gnn_ln1_b, L0_gnn_Wl, L0_gnn_Wr, L0_gnn_att, L0_gnn_gat_bias, L0_gnn_ln2_g, L0_gnn_ln2_b, L0_gnn_W1, L0_gnn_b1, L0_gnn_W2, L0_gnn_b2, L1_gnn_Wp0, L1_gnn_bp0, L1_gnn_Wl0, L1_gnn_bl0, L1_gnn_Wr0, L1_gnn_g0, L1_gnn_be0, L1_gnn_Wp1, L1_gnn_bp1, L1_gnn_Wl1, L1_gnn_bl1, L1_gnn_Wr1, L1_gnn_g1, L1_gnn_be1, L1_gnn_Wp2, L1_gnn_bp2, L1_gnn_Wl2, L1_gnn_bl2, L1_gnn_Wr2):
    import jax
    import jax.numpy as jnp

    def _L0_gnn_ref(x, edge_index, ln1_g, ln1_b, Wl, Wr, att, gat_bias, ln2_g, ln2_b, W1, b1, W2, b2):
        import jax, jax.numpy as jnp
        import numpy as np
        N_EMBD = 512
        HEADS = 8
        C = N_EMBD // HEADS
        N_NODES = 1250
        N_EDGES = 20000
        NEG_SLOPE = 0.2
        LN_EPS = 1e-05

        def _layer_norm(x, g, b):
            mu = jnp.mean(x, axis=-1, keepdims=True)
            var = jnp.mean(jnp.square(x - mu), axis=-1, keepdims=True)
            return (x - mu) * jax.lax.rsqrt(var + LN_EPS) * g + b

        def _gatv2(x, edge_index, Wl, Wr, att, gat_bias):
            src, dst = (edge_index[0], edge_index[1])
            xl = (x @ Wl).reshape(-1, HEADS, C)
            xr = (x @ Wr).reshape(-1, HEADS, C)
            h = jax.nn.leaky_relu(xl[src] + xr[dst], NEG_SLOPE)
            e = jnp.einsum('ehc,hc->eh', h, att)
            m = jax.ops.segment_max(e, dst, num_segments=N_NODES)
            ex = jnp.exp(e - m[dst])
            denom = jax.ops.segment_sum(ex, dst, num_segments=N_NODES)
            alpha = ex / (denom[dst] + 1e-16)
            msg = alpha[..., None] * xl[src]
            out = jax.ops.segment_sum(msg, dst, num_segments=N_NODES)
            return out.reshape(-1, HEADS * C) + gat_bias
        h = _layer_norm(x, ln1_g, ln1_b)
        h = _gatv2(h, edge_index, Wl, Wr, att, gat_bias)
        x = x + h
        h = _layer_norm(x, ln2_g, ln2_b)
        h = jax.nn.gelu(h @ W1 + b1, approximate=False) @ W2 + b2
        return x + h

    def _L1_gnn_ref(x, edge_index, Wp0, bp0, Wl0, bl0, Wr0, g0, be0, Wp1, bp1, Wl1, bl1, Wr1, g1, be1, Wp2, bp2, Wl2, bl2, Wr2):
        import jax, jax.numpy as jnp
        import numpy as np
        N = 1250
        E = 20000
        D = 512
        EPS = 1e-05

        def _lin_params(key, out_d, in_d, bias=True):
            k1, k2 = jax.random.split(key)
            s = 1.0 / np.sqrt(in_d)
            W = jax.random.uniform(k1, (out_d, in_d), jnp.float32, -s, s)
            if bias:
                b = jax.random.uniform(k2, (out_d,), jnp.float32, -s, s)
                return (W, b)
            return (W,)

        def _sage_conv(x, src, dst, Wp, bp, Wl, bl, Wr):
            h = jax.nn.relu(x @ Wp.T + bp)
            agg = jax.ops.segment_sum(h[src], dst, num_segments=N)
            cnt = jax.ops.segment_sum(jnp.ones((src.shape[0],), x.dtype), dst, num_segments=N)
            agg = agg / jnp.maximum(cnt, 1.0)[:, None]
            return agg @ Wl.T + bl + x @ Wr.T

        def _relu_ln(x, g, b):
            x = jax.nn.relu(x)
            mu = jnp.mean(x, axis=-1, keepdims=True)
            var = jnp.mean(jnp.square(x - mu), axis=-1, keepdims=True)
            return (x - mu) * jax.lax.rsqrt(var + EPS) * g + b
        src, dst = (edge_index[0], edge_index[1])
        x = _sage_conv(x, src, dst, Wp0, bp0, Wl0, bl0, Wr0)
        x = _relu_ln(x, g0, be0)
        x = _sage_conv(x, src, dst, Wp1, bp1, Wl1, bl1, Wr1)
        x = _relu_ln(x, g1, be1)
        x = _sage_conv(x, src, dst, Wp2, bp2, Wl2, bl2, Wr2)
        return x
    edge_index = jnp.stack([src, dst])
    x = _layernorm(x + _L0_gnn_ref(x, edge_index, L0_gnn_ln1_g, L0_gnn_ln1_b, L0_gnn_Wl, L0_gnn_Wr, L0_gnn_att, L0_gnn_gat_bias, L0_gnn_ln2_g, L0_gnn_ln2_b, L0_gnn_W1, L0_gnn_b1, L0_gnn_W2, L0_gnn_b2), axis=-1)
    x = _layernorm(x + _L1_gnn_ref(x, edge_index, L1_gnn_Wp0, L1_gnn_bp0, L1_gnn_Wl0, L1_gnn_bl0, L1_gnn_Wr0, L1_gnn_g0, L1_gnn_be0, L1_gnn_Wp1, L1_gnn_bp1, L1_gnn_Wl1, L1_gnn_bl1, L1_gnn_Wr1, L1_gnn_g1, L1_gnn_be1, L1_gnn_Wp2, L1_gnn_bp2, L1_gnn_Wl2, L1_gnn_bl2, L1_gnn_Wr2), axis=-1)
    return x

_drawn_inputs = setup_inputs


def setup_inputs(seed=0):
    import zlib

    import numpy as np

    out = dict(_drawn_inputs(seed))
    spreads = {'L0_gnn_ln1_g': (1.0, 0.6),
     'L0_gnn_ln1_b': (0.0, 0.302),
     'L0_gnn_gat_bias': (0.0, 0.1),
     'L0_gnn_ln2_g': (1.0, 0.6),
     'L0_gnn_ln2_b': (0.0, 0.556),
     'L0_gnn_b1': (0.0, 0.267),
     'L0_gnn_b2': (0.0, 0.1),
     'L1_gnn_g0': (1.0, 0.2),
     'L1_gnn_be0': (0.0, 0.1),
     'L1_gnn_g1': (1.0, 0.2),
     'L1_gnn_be1': (0.0, 0.1)}
    factors = {'L0_gnn_Wr': 8.0,
     'L0_gnn_att': 8.0,
     'L1_gnn_bp0': 5.821,
     'L1_gnn_bp1': 6.882,
     'L1_gnn_bp2': 7.996,
     'L1_gnn_bl2': 2.714}
    for name, (base, spread) in spreads.items():
        noise = np.random.default_rng([zlib.crc32(name.encode()), seed]).standard_normal(out[name].shape)
        drawn = base * np.exp(spread * noise) if base else spread * noise
        out[name] = jnp.asarray(drawn.astype(out[name].dtype))
    for name, factor in factors.items():
        out[name] = (out[name] * factor).astype(out[name].dtype)
    return out
```

```python
import concourse.bass as bass
from concourse import mybir
from contextlib import ExitStack

FP32 = mybir.dt.float32
BF16 = mybir.dt.bfloat16
I32 = mybir.dt.int32
I16 = mybir.dt.int16
ALU = mybir.AluOpType
ACT = mybir.ActivationFunctionType
AX = mybir.AxisListType

N = 1250
D = 512
HEADS = 8
C = D // HEADS
E = 40000
FF = 4 * D
EPS = 1e-5

P = 125
NT = N // P
CK = D // 128

KG = 4
GE = KG * 128
EG = -(-E // GE)
EGP = EG + 1
NG = EG + NT - 1
NGP = NG + 8
NV = NG * KG
HALF = D // 2 + HEADS // 2
ROW = 2 * HALF
PAD_DST = 1 << 20
KEY_STEP = 2048
BIG = 1e30
QG = NV // 16
assert N % P == 0 and NG % 2 == 0 and NV % 16 == 0


def linker(engine, sem):
    count = [0]

    def link(instruction):
        count[0] += 1
        instruction.then_inc(sem, 1)
        engine.wait_ge(sem, count[0])

    return link


def row_view(ap):
    return ap.rearrange("(a n) -> a n", a=1)


class Core:

    def __init__(self, nc, ctx):
        self.nc, self.ctx = nc, ctx
        self.n = 0
        self.sems = []

    def sem(self, name):
        self.n += 1
        self.sems.append(self.nc.alloc_semaphore(f"{name}_{self.n}"))
        return self.sems[-1]

    def recycle(self):
        self.nc.clear_and_free_semaphores(self.sems)
        self.sems = []
        self.nc.all_engine_barrier()

    def sb(self, scope, name, shape, dt=FP32):
        self.n += 1
        return scope.enter_context(self.nc.sbuf_tensor(f"{name}_{self.n}", shape, dt))

    def ps(self, scope, name, shape, dt=FP32):
        self.n += 1
        return scope.enter_context(self.nc.psum_tensor(f"{name}_{self.n}", shape, dt))


def setup_constants(core, ident, iota_node, iota_row, iota_row16):
    nc = core.nc
    sem = core.sem("constants_built")
    with nc.Block() as block:
        @block.gpsimd
        def _(pool):
            link = linker(pool, sem)
            link(nc.gpsimd.memset(ident[:, :], 0.0))
            link(nc.gpsimd.affine_select(out=ident[:, :], in_=ident[:, :], compare_op=ALU.not_equal, fill=1.0,
                                         base=0, pattern=[[-1, 128]], channel_multiplier=1))
            link(nc.gpsimd.iota(iota_node[:, :], [[0, 1]], base=0, channel_multiplier=1,
                                allow_small_or_imprecise_dtypes=True))
            link(nc.gpsimd.iota(iota_row[:, :], [[1, P]], base=0, channel_multiplier=0,
                                allow_small_or_imprecise_dtypes=True))
            link(nc.gpsimd.iota(iota_row16[:, :], [[1, N]], base=0, channel_multiplier=0,
                                allow_small_or_imprecise_dtypes=True))


def order_edges(core, src, dst, ident, dst_f, edges_dram):
    nc = core.nc
    BINS = N + 1
    TILES = EGP * KG
    full = EG - 1
    rest = E - full * GE
    banks = [(0, 512), (512, 512), (1024, BINS - 1024)]
    with ExitStack() as scope:
        sb = lambda name, shape, dt=FP32: core.sb(scope, name, shape, dt)
        rows = sb("rows", [EGP, 2, GE], I32)
        pairs = sb("pairs", [EGP, GE, 2], I32)
        after = sb("after", [EGP, 1], I32)
        after_f = sb("after_f", [EGP, 1])
        src_f = sb("src_f", [EGP, GE])
        drops = sb("drops", [EGP, GE])
        row_drops = sb("row_drops", [EGP, 1])
        ones = sb("ones", [128, 128])
        flag = sb("flag", [1, 1], I32)
        srcT = sb("srcT", [128, EGP, KG])
        dstT = sb("dstT", [128, EGP, KG])
        binT = sb("binT", [128, TILES])
        bins = sb("bins", [128, BINS], I16)
        before = sb("before", [128, 128], BF16)
        ones_b = sb("ones_b", [128, 128], BF16)
        hot = sb("hot", [128, BINS], BF16)
        nxt = sb("next_place", [128, BINS])
        ones_row = sb("ones_row", [128, BINS])
        zero_b = sb("zero_b", [128, 512], BF16)
        sel = sb("sel", [128, BINS])
        place = sb("place", [128, 1])
        place_i = sb("place_i", [128, 1], I32)
        pair = sb("pair", [128, 2], I32)
        lower = core.ps(scope, "lower", [128, 3, 512])
        total = core.ps(scope, "total", [128, 3, 512])
        tp = core.ps(scope, "tp", [128, 128])
        padded, loaded, laid, stored = core.sem("padded"), core.sem("loaded"), core.sem("pairs_laid"), core.sem("stored")
        counted, summed, flagged = core.sem("counted"), core.sem("summed"), core.sem("flagged")
        dve, pe_tp, copied = core.sem("dve_steps"), core.sem("tile_transposed"), core.sem("tile_copied")
        sort_ready, hot_made, hist_added, hist_done = (core.sem(n) for n in ("sort_ready", "hot_made", "hist_added", "hist_done"))
        ranked, chain, placed, scattered, begun = (core.sem(n) for n in ("ranked", "chain", "placed", "scattered", "begun"))
        dve_end, cleared, gone = core.sem("dve_end"), core.sem("cleared"), core.sem("gone")
        with nc.Block() as block:
            @block.gpsimd
            def _(pool):
                nc.gpsimd.memset(rows[:, 0, :], 0).then_inc(padded, 1)
                nc.gpsimd.memset(rows[:, 1, :], PAD_DST).then_inc(padded, 1)
                nc.gpsimd.memset(after[:, :], PAD_DST).then_inc(padded, 1)
                pool.wait_ge(flagged, 1)
                unordered = pool.value_load(flag[0:1, 0:1], min_val=0, max_val=E)
                with pool.If(unordered > 0):
                    nc.gpsimd.memset(before[:, :], 0.0).then_inc(cleared, 1)
                    pool.wait_ge(cleared, 1)
                    nc.gpsimd.affine_select(out=before[:, :], in_=before[:, :], compare_op=ALU.is_ge, fill=1.0, base=0,
                                            pattern=[[-1, 128]], channel_multiplier=1).then_inc(sort_ready, 1)
                    nc.gpsimd.iota(bins[:, :], [[1, BINS]], base=0, channel_multiplier=0,
                                   allow_small_or_imprecise_dtypes=True).then_inc(sort_ready, 1)
                    pool.wait_ge(stored, 16)
                    with pool.Fori(0, TILES) as t:
                        pool.wait_ge(placed, t + 1)
                        pool.sem_inc(begun, 1)
                        nc.gpsimd.indirect_dma_start(edges_dram.rearrange("g (e a) -> (g e) a", a=2),
                                                     bass.IndirectOffsetOnAxis(ap=place_i[:, 0:1], axis=0),
                                                     pair[:, :], None).then_inc(scattered, 16)
                        pool.wait_ge(scattered, 16 * t + 16)
                        pool.sem_inc(gone, 1)
                    pool.sem_inc(begun, 1)

            @block.sync
            def _(sp):
                sp.wait_ge(padded, 3)
                for a, e in ((0, src), (1, dst)):
                    sp.dma_start(rows[0:full, a, :], e[0:full * GE].rearrange("(g e) -> g e", e=GE)).then_inc(loaded, 16)
                    sp.dma_start(rows[full:EG, a, 0:rest], row_view(e[full * GE:E])).then_inc(loaded, 16)
                sp.dma_start(after[0:full - 1, :], dst[GE:full * GE].rearrange("(g e) -> g e", e=GE)[:, 0:1],
                             allow_slow_non_contiguous=True).then_inc(loaded, 16)
                sp.dma_start(after[full - 1:full, :], row_view(dst[full * GE:full * GE + 1])).then_inc(loaded, 16)
                sp.wait_ge(laid, 2)
                sp.dma_start(edges_dram, pairs[:, :, :].rearrange("p e a -> p (e a)")).then_inc(stored, 16)
                sp.wait_ge(stored, 16)

            @block.tensor
            def _(pe):
                pe.wait_ge(counted, 1)
                nc.tensor.matmul(total[:, 0, 0:1], ones[0:EGP, :], row_drops[:, :], start=True, stop=True).then_inc(summed, 1)
                pe.wait_ge(flagged, 1)
                unordered = pe.value_load(flag[0:1, 0:1], min_val=0, max_val=E)
                with pe.If(unordered > 0):
                    n = 0
                    for of in (src_f, dst_f):
                        for k in range(KG):
                            if n:
                                pe.wait_ge(copied, n)
                            nc.tensor.transpose(tp[:, 0:EGP], of[:, k * 128:(k + 1) * 128], ident[0:EGP, 0:EGP]).then_inc(pe_tp, 1)
                            n += 1
                    pe.wait_ge(sort_ready, 6)
                    for q, (c0, cn) in enumerate(banks):
                        nc.tensor.matmul(total[:, q, 0:cn], ones_b[:, :], zero_b[:, 0:cn], start=True, stop=True)
                    with pe.Fori(0, TILES) as t:
                        pe.wait_ge(hot_made, t + 1)
                        for q, (c0, cn) in enumerate(banks):
                            last = nc.tensor.matmul(total[:, q, 0:cn], ones_b[:, :], hot[:, c0:c0 + cn],
                                                    start=False, stop=True, skip_group_check=True)
                        last.then_inc(hist_added, 1)
                    pe.wait_ge(hist_done, 1)
                    with pe.Fori(0, TILES) as t:
                        pe.wait_ge(hot_made, t + (TILES + 1))
                        for q, (c0, cn) in enumerate(banks):
                            nc.tensor.matmul(lower[:, q, 0:cn], before[:, :], hot[:, c0:c0 + cn], start=True, stop=True)
                            last = nc.tensor.matmul(total[:, q, 0:cn], ones_b[:, :], hot[:, c0:c0 + cn], start=True, stop=True)
                        last.then_inc(ranked, 1)
                    pe.sem_inc(begun, 1)

            @block.vector
            def _(v):
                link = linker(v, dve)
                link(nc.vector.memset(ones[:, :], 1.0))
                v.wait_ge(loaded, 96)
                for a in range(2):
                    nc.vector.tensor_copy(pairs[:, :, a], rows[:, a, :]).then_inc(laid, 1)
                link(nc.vector.tensor_copy(dst_f[:, :], rows[:, 1, :]))
                link(nc.vector.tensor_copy(src_f[:, :], rows[:, 0, :]))
                link(nc.vector.tensor_copy(after_f[:, :], after[:, :]))
                link(nc.vector.tensor_tensor(drops[:, 0:GE - 1], dst_f[:, 0:GE - 1], dst_f[:, 1:GE], ALU.is_gt))
                link(nc.vector.tensor_tensor(drops[:, GE - 1:GE], dst_f[:, GE - 1:GE], after_f[:, :], ALU.is_gt))
                nc.vector.tensor_reduce(row_drops[:, :], drops[:, :], AX.X, ALU.add).then_inc(counted, 1)
                v.wait_ge(summed, 1)
                nc.vector.tensor_copy(flag[:, :], total[0:1, 0, 0:1]).then_inc(flagged, 1)
                v.wait_ge(flagged, 1)
                unordered = v.value_load(flag[0:1, 0:1], min_val=0, max_val=E)
                with v.If(unordered > 0):
                    n = 0
                    for to in (srcT, dstT):
                        for k in range(KG):
                            v.wait_ge(pe_tp, n + 1)
                            nc.vector.tensor_copy(to[:, :, k], tp[:, 0:EGP]).then_inc(copied, 1)
                            n += 1
                    v.wait_ge(copied, n)
                    nc.vector.memset(ones_b[:, :], 1.0).then_inc(sort_ready, 1)
                    nc.vector.memset(zero_b[:, :], 0.0).then_inc(sort_ready, 1)
                    nc.vector.memset(ones_row[:, :], 1.0).then_inc(sort_ready, 1)
                    nc.vector.tensor_scalar(binT[:, :], dstT[:, :, :].rearrange("p g k -> p (g k)"), float(N), None,
                                            ALU.min).then_inc(sort_ready, 1)
                    v.wait_ge(sort_ready, 6)
                    v.sem_inc(hist_added, 1)
                    with v.Fori(0, TILES) as t:
                        v.wait_ge(hist_added, t + 1)
                        nc.vector.tensor_scalar(hot[:, :], bins[:, :], binT[:, bass.ds(t, 1)], None, ALU.is_equal).then_inc(hot_made, 1)
                    v.wait_ge(hist_added, TILES + 1)
                    for q, (c0, cn) in enumerate(banks):
                        nc.vector.tensor_copy(sel[:, c0:c0 + cn], total[:, q, 0:cn]).then_inc(chain, 1)
                    v.wait_ge(chain, 3)
                    nc.vector.tensor_tensor_scan(nxt[:, :], ones_row[:, :], sel[:, :], 0.0, ALU.mult, ALU.add).then_inc(chain, 1)
                    v.wait_ge(chain, 4)
                    nc.vector.tensor_tensor(nxt[:, :], nxt[:, :], sel[:, :], ALU.subtract).then_inc(chain, 1)
                    v.wait_ge(chain, 5)
                    v.sem_inc(hist_done, 1)
                    v.sem_inc(gone, 1)
                    with v.Fori(0, TILES) as t:
                        nc.vector.tensor_scalar(hot[:, :], bins[:, :], binT[:, bass.ds(t, 1)], None, ALU.is_equal).then_inc(hot_made, 1)
                        v.wait_ge(ranked, t + 1)
                        for q, (c0, cn) in enumerate(banks):
                            nc.vector.tensor_tensor(sel[:, c0:c0 + cn], nxt[:, c0:c0 + cn], lower[:, q, 0:cn], ALU.add).then_inc(chain, 1)
                        v.wait_ge(chain, 10 * t + 8)
                        nc.vector.tensor_tensor(sel[:, :], sel[:, :], hot[:, :], ALU.mult).then_inc(chain, 1)
                        for q, (c0, cn) in enumerate(banks):
                            nc.vector.tensor_tensor(nxt[:, c0:c0 + cn], nxt[:, c0:c0 + cn], total[:, q, 0:cn], ALU.add).then_inc(chain, 1)
                        v.wait_ge(chain, 10 * t + 12)
                        nc.vector.tensor_reduce(place[:, :], sel[:, :], AX.X, ALU.add).then_inc(chain, 1)
                        v.wait_ge(chain, 10 * t + 13)
                        v.wait_ge(gone, t + 1)
                        nc.vector.tensor_copy(pair[:, 0:1], srcT[:, :, :].rearrange("p g k -> p (g k)")[:, bass.ds(t, 1)]).then_inc(chain, 1)
                        nc.vector.tensor_copy(pair[:, 1:2], dstT[:, :, :].rearrange("p g k -> p (g k)")[:, bass.ds(t, 1)]).then_inc(chain, 1)
                        v.wait_ge(chain, 10 * t + 15)
                        nc.vector.tensor_copy(place_i[:, :], place[:, :]).then_inc(placed, 1)
                        v.wait_ge(placed, t + 1)
                        v.sem_inc(dve_end, 1)
                    v.sem_inc(dve_end, 1)


def plan_visits(core, dst_f, ident, srcT_i, srcT_f, dlT, visit_table, edges_dram, dloc_dram, key_dram):
    nc = core.nc
    with ExitStack() as scope:
        sb = lambda name, shape, dt=FP32: core.sb(scope, name, shape, dt)
        ps = lambda name, shape, dt=FP32: core.ps(scope, name, shape, dt)
        W = NG + 1
        below = sb("below", [EGP, GE])
        counts = sb("counts", [EGP, NT - 1])
        ones = sb("ones", [128, 128])
        starts = sb("starts", [128, NT + 1])
        starts_up = sb("starts_up", [128, NT])
        lo_i = sb("lo_i", [128, NT + 1], I32)
        hi_i = sb("hi_i", [128, NT], I32)
        lo = sb("lo", [128, NT])
        hi = sb("hi", [128, NT])
        n_vis = sb("n_vis", [128, NT])
        ones_nt = sb("ones_nt", [128, NT])
        base = sb("base", [128, NT + 1])
        shift = sb("shift", [128, NT])
        dshift = sb("dshift", [128, NT])
        v_iota = sb("v_iota", [128, W])
        bucket = sb("bucket", [128, W])
        group = sb("group", [128, W])
        step = sb("step", [128, W])
        group_i = sb("group_i", [128, 1], I32)
        table_f = sb("table_f", [1, 3, NG])
        vis_i = sb("vis_i", [NGP, GE, 2], I32)
        vis_f = sb("vis_f", [NGP, 2, GE])
        key = sb("key", [NGP, GE])
        off = sb("off", [128, 1])
        key_off = sb("key_off", [128, 1])
        dloc = sb("dloc", [NGP, GE])
        dloc_c = sb("dloc_c", [NGP, GE], BF16)
        sums = ps("sums", [128, 512])
        tp = ps("tp", [128, 2, KG, 128])
        memset_done = core.sem("iota_written")
        dve = core.sem("plan_steps")
        counted = core.sem("counts_ready")
        summed = core.sem("sums_ready")
        group_ready = core.sem("group_index_ready")
        gathered = core.sem("visits_gathered")
        vis_ready = core.sem("visit_rows_ready")
        transposed = core.sem("visit_rows_transposed")
        stored = core.sem("visit_rows_stored")
        with nc.Block() as block:
            @block.gpsimd
            def _(pool):
                nc.gpsimd.iota(v_iota[:, 0:NG], [[1, NG]], base=0, channel_multiplier=0,
                               allow_small_or_imprecise_dtypes=True).then_inc(memset_done, 1)
                nc.gpsimd.iota(v_iota[:, NG:W], [[0, 1]], base=0, channel_multiplier=1,
                               allow_small_or_imprecise_dtypes=True).then_inc(memset_done, 1)
                pool.wait_ge(group_ready, 1)
                nc.gpsimd.indirect_dma_start(vis_i[:, :, :].rearrange("p a b -> p (a b)"), None, edges_dram,
                                             bass.IndirectOffsetOnAxis(ap=group_i[0:NGP, 0:1], axis=0)
                                             ).then_inc(gathered, 16)

            @block.sync
            def _(sp):
                sp.wait_ge(vis_ready, 1)
                sp.dma_start(key_dram, key[:, :]).then_inc(stored, 16)
                sp.dma_start(dloc_dram, dloc_c[:, :]).then_inc(stored, 16)
                sp.wait_ge(stored, 32)

            @block.tensor
            def _(pe):
                pe.wait_ge(counted, 1)
                nc.tensor.matmul(sums[:, 0:NT - 1], ones[0:EGP, :], counts[:, :], start=True, stop=True).then_inc(summed, 1)
                pe.wait_ge(vis_ready, 1)
                for a, rows in ((0, vis_f[0:NG, 0, :]), (1, dloc[0:NG, :])):
                    for k in range(KG):
                        last = nc.tensor.transpose(tp[:, a, k, 0:NG], rows[:, k * 128:(k + 1) * 128], ident[0:NG, 0:NG])
                last.then_inc(transposed, 1)

            @block.vector
            def _(v):
                link = linker(v, dve)
                link(nc.vector.memset(ones[:, :], 1.0))
                link(nc.vector.memset(ones_nt[:, :], 1.0))
                for b in range(1, NT):
                    link(nc.vector.tensor_scalar(below[:, :], dst_f[:, :], float(P * b), None, ALU.is_lt, ALU.add,
                                                 accum_out=counts[:, b - 1:b]))
                nc.vector.memset(starts[:, 0:1], 0.0).then_inc(counted, 1)
                link(nc.vector.memset(starts[:, NT:NT + 1], float(E)))
                v.wait_ge(summed, 1)
                link(nc.vector.tensor_copy(starts[:, 1:NT], sums[:, 0:NT - 1]))
                v.wait_ge(counted, 1)
                link(nc.vector.tensor_scalar(starts_up[:, :], starts[:, 1:NT + 1], float(GE - 1), None, ALU.add))
                link(nc.vector.tensor_copy(lo_i[:, :], starts[:, :]))
                link(nc.vector.tensor_copy(hi_i[:, :], starts_up[:, :]))
                link(nc.vector.tensor_scalar(lo_i[:, :], lo_i[:, :], 9, None, ALU.logical_shift_right))
                link(nc.vector.tensor_scalar(hi_i[:, :], hi_i[:, :], 9, None, ALU.logical_shift_right))
                link(nc.vector.tensor_copy(lo[:, :], lo_i[:, 0:NT]))
                link(nc.vector.tensor_copy(hi[:, :], hi_i[:, :]))
                link(nc.vector.tensor_tensor(n_vis[:, :], hi[:, :], lo[:, :], ALU.subtract))
                link(nc.vector.tensor_scalar(n_vis[:, :], n_vis[:, :], 1.0, None, ALU.max))
                link(nc.vector.memset(base[:, 0:1], 0.0))
                link(nc.vector.tensor_tensor_scan(base[:, 1:NT + 1], ones_nt[:, :], n_vis[:, :], 0.0, ALU.mult, ALU.add))
                link(nc.vector.tensor_tensor(shift[:, :], lo[:, :], base[:, 0:NT], ALU.subtract))
                link(nc.vector.tensor_tensor(dshift[:, 1:NT], shift[:, 1:NT], shift[:, 0:NT - 1], ALU.subtract))
                v.wait_ge(memset_done, 2)
                link(nc.vector.tensor_scalar(group[:, :], v_iota[:, :], shift[:, 0:1], None, ALU.add))
                link(nc.vector.memset(bucket[:, :], 0.0))
                for b in range(1, NT):
                    link(nc.vector.scalar_tensor_tensor(bucket[:, :], v_iota[:, :], base[:, b:b + 1], bucket[:, :],
                                                        ALU.is_ge, ALU.add))
                    link(nc.vector.tensor_scalar(step[:, :], v_iota[:, :], base[:, b:b + 1], dshift[:, b:b + 1],
                                                 ALU.is_ge, ALU.mult))
                    link(nc.vector.tensor_tensor(group[:, :], group[:, :], step[:, :], ALU.add))
                link(nc.vector.tensor_scalar(group[:, :], group[:, :], float(EGP - 1), None, ALU.min))
                nc.vector.tensor_copy(group_i[:, :], group[:, NG:W]).then_inc(group_ready, 1)
                link(nc.vector.tensor_copy(table_f[:, 0, :], bucket[0:1, 0:NG]))
                link(nc.vector.memset(table_f[:, 1:3, :], 1.0))
                link(nc.vector.tensor_tensor(table_f[:, 1, 1:NG], bucket[0:1, 1:NG], bucket[0:1, 0:NG - 1], ALU.not_equal))
                link(nc.vector.tensor_tensor(table_f[:, 2, 0:NG - 1], bucket[0:1, 1:NG], bucket[0:1, 0:NG - 1], ALU.not_equal))
                link(nc.vector.tensor_copy(visit_table[:, :, :], table_f[:, :, :]))
                link(nc.vector.tensor_scalar(off[:, :], bucket[:, NG:W], float(P), None, ALU.mult))
                link(nc.vector.tensor_scalar(key_off[:, :], bucket[:, NG:W], float(KEY_STEP), None, ALU.mult))
                v.wait_ge(gathered, 16)
                link(nc.vector.tensor_copy(vis_f[:, :, :], vis_i[:, :, :].rearrange("p e a -> p a e")))
                link(nc.vector.tensor_scalar(key[:, :], vis_f[:, 1, :], key_off[0:NGP, :], None, ALU.add))
                link(nc.vector.tensor_scalar(dloc[:, :], vis_f[:, 1, :], off[0:NGP, :], None, ALU.subtract))
                link(nc.vector.tensor_scalar(dloc[:, :], dloc[:, :], -1.0, float(P), ALU.max, ALU.min))
                nc.vector.tensor_copy(dloc_c[:, :], dloc[:, :]).then_inc(vis_ready, 1)
                v.wait_ge(transposed, 1)
                by_visit = lambda a: tp[:, a, :, 0:NG].rearrange("p k g -> p g k")
                link(nc.vector.tensor_copy(srcT_i[:, :].rearrange("p (g k) -> p g k", k=KG), by_visit(0)))
                link(nc.vector.tensor_copy(srcT_f[:, :].rearrange("p (g k) -> p g k", k=KG), by_visit(0)))
                link(nc.vector.tensor_copy(dlT[:, :].rearrange("p (g k) -> p g k", k=KG), by_visit(1)))


def load_block(core, pairs, broadcasts=()):
    nc = core.nc
    sem = core.sem("loaded")
    with nc.Block() as block:
        @block.sync
        def _(sp):
            for to, of in pairs:
                sp.dma_start(to, of).then_inc(sem, 16)
            sp.wait_ge(sem, 16 * len(pairs))


def norm_block(core, X, XT, ident, gain=None, bias=None, normed=None, out=None, relu=False):
    nc = core.nc
    with ExitStack() as scope:
        stats = core.sb(scope, "stats", [P, NT, 6])
        mv = core.sb(scope, "mean_var", [P, NT, 2])
        ve = core.sb(scope, "var_eps", [P, NT])
        sd = core.sb(scope, "deviation", [P, NT])
        rstd = core.sb(scope, "rstd", [P, NT])
        work = normed if normed is not None else core.sb(scope, "xn", [P, 2, D])
        slots = NT if normed is not None else 2
        tp = [core.ps(scope, "tp", [128, CK, P]) for _ in range(2)]
        stat_done, aggr_done = core.sem("stats_done"), core.sem("aggregated")
        var_ready, sd_ready, rstd_ready = core.sem("var_ready"), core.sem("sd_ready"), core.sem("rstd_ready")
        normed_done, tp_done, evac_done = core.sem("normed"), core.sem("transposed"), core.sem("evacuated")
        stored = core.sem("out_stored")
        with nc.Block() as block:
            @block.vector
            def _(v):
                for t in range(NT):
                    nc.vector.bn_stats(stats[:, t, :], X[:, t, :]).then_inc(stat_done, 1)
                for t in range(NT):
                    v.wait_ge(stat_done, t + 1)
                    nc.vector.bn_aggr(mv[:, t, :], stats[:, t, :]).then_inc(aggr_done, 1)
                v.wait_ge(aggr_done, NT)
                nc.vector.tensor_scalar(ve[:, :], mv[:, :, 1], EPS, None, ALU.add).then_inc(var_ready, 1)
                v.wait_ge(sd_ready, 1)
                nc.vector.reciprocal(rstd[:, :], sd[:, :]).then_inc(rstd_ready, 1)
                v.wait_ge(rstd_ready, 1)
                for t in range(NT):
                    if XT is not None and t >= slots:
                        v.wait_ge(tp_done, t - slots + 1)
                    nc.vector.tensor_scalar(work[:, t % slots, :], X[:, t, :], mv[:, t, 0:1], rstd[:, t:t + 1],
                                            ALU.subtract, ALU.mult).then_inc(normed_done, 1)

            @block.scalar
            def _(act):
                act.wait_ge(var_ready, 1)
                nc.scalar.activation(sd[:, :], ve[:, :], ACT.Sqrt).then_inc(sd_ready, 1)
                if XT is not None:
                    for t in range(NT):
                        act.wait_ge(tp_done, t + 1)
                        cols = slice(t * P, (t + 1) * P)
                        if gain is None:
                            nc.scalar.activation(XT[:, :, cols], tp[t % 2][:, :, :], ACT.Copy).then_inc(evac_done, 1)
                        else:
                            for c in range(CK):
                                last = nc.scalar.activation(XT[:, c, cols], tp[t % 2][:, c, :], ACT.Identity,
                                                            scale=gain[:, c:c + 1], bias=bias[:, c:c + 1])
                            last.then_inc(evac_done, 1)

            if XT is not None:
                @block.tensor
                def _(pe):
                    for t in range(NT):
                        pe.wait_ge(normed_done, t + 1)
                        if t >= 2:
                            pe.wait_ge(evac_done, t - 1)
                        for c in range(CK):
                            last = nc.tensor.transpose(tp[t % 2][:, c, :], work[:, t % slots, c * 128:(c + 1) * 128],
                                                       ident[0:P, 0:P])
                        last.then_inc(tp_done, 1)

            if out is not None:
                @block.sync
                def _(sp):
                    for t in range(NT):
                        sp.wait_ge(normed_done, t + 1)
                        sp.dma_start(out[t * P:(t + 1) * P, :], work[:, t, :]).then_inc(stored, 16)
                    sp.wait_ge(stored, 16 * NT)


def build_tables(core, hT, Wl, Wr, att_row, lin_row, xl_dram, xr_parts):
    nc = core.nc
    with ExitStack() as scope:
        rows = core.sb(scope, "rows", [P, 2, 2, 2, HALF])
        prod = core.sb(scope, "prod", [P, 2, D])
        resid = core.sb(scope, "resid", [P, 2, 2, HALF])
        acc = [[core.ps(scope, "acc", [P, D]) for _ in range(2)] for _ in range(2)]
        mm_done, copied, lin_done = core.sem("product_done"), core.sem("row_copied"), core.sem("linear_done")
        prod_done, stored = core.sem("prod_done"), [core.sem("row_stored"), core.sem("row_stored")]
        part_done, resid_done = core.sem("part_done"), core.sem("resid_done")

        def heads(ap):
            return ap[:, :, 0:D // 2].rearrange("p a (h c) -> p a h c", c=C)

        with nc.Block() as block:
            @block.tensor
            def _(pe):
                for t in range(NT):
                    for s, w in ((0, Wl), (1, Wr)):
                        if t >= 2:
                            pe.wait_ge(copied, 2 * (t - 2) + s + 1)
                        for k in range(CK):
                            last = nc.tensor.matmul(acc[t % 2][s][:, :], hT[:, k, t * P:(t + 1) * P], w[:, k, :],
                                                    start=(k == 0), stop=(k == CK - 1))
                        last.then_inc(mm_done, 1)

            @block.scalar
            def _(act):
                for t in range(NT):
                    sl = t % 2
                    for s in range(2):
                        act.wait_ge(mm_done, 2 * t + s + 1)
                        if t >= 2 and s == 0:
                            act.wait_ge(stored[sl], 16 * (t // 2))
                        if t >= 2 and s == 1:
                            act.wait_ge(resid_done, 2 * (t - 2) + 1)
                        if t >= 2:
                            act.wait_ge(lin_done, 2 * (t - 2) + s + 1)
                        nc.scalar.activation(rows[:, sl, s, :, 0:D // 2],
                                             acc[sl][s][:, :].rearrange("p (a c) -> p a c", a=2),
                                             ACT.Copy).then_inc(copied, 1)
                    act.wait_ge(lin_done, 2 * t + 2)
                    nc.scalar.activation(xr_parts[:, t, 0, :, :], rows[:, sl, 1, :, :], ACT.Copy).then_inc(part_done, 1)
                    act.wait_ge(resid_done, 2 * t + 1)
                    nc.scalar.activation(xr_parts[:, t, 1, :, :], resid[:, 0, :, :], ACT.Copy).then_inc(part_done, 1)
                    act.wait_ge(resid_done, 2 * t + 2)
                    nc.scalar.activation(xr_parts[:, t, 2, :, :], resid[:, 1, :, :], ACT.Copy).then_inc(part_done, 1)

            @block.vector
            def _(v):
                for t in range(NT):
                    sl = t % 2
                    for s in range(2):
                        v.wait_ge(copied, 2 * t + s + 1)
                        if t > 0 or s > 0:
                            v.wait_ge(lin_done, 2 * t + s)
                        nc.vector.tensor_tensor(prod[:, s, :].rearrange("p (a c) -> p a c", a=2),
                                                rows[:, sl, s, :, 0:D // 2],
                                                lin_row[:, :].rearrange("p (a c) -> p a c", a=2),
                                                ALU.mult).then_inc(prod_done, 1)
                        v.wait_ge(prod_done, 2 * t + s + 1)
                        nc.vector.tensor_reduce(rows[:, sl, s, :, D // 2:HALF],
                                                prod[:, s, :].rearrange("p (a h c) -> p a h c", a=2, c=C),
                                                AX.X, ALU.add).then_inc(lin_done, 1)
                    v.wait_ge(part_done, 3 * t + 1)
                    nc.vector.tensor_tensor(resid[:, 0, :, :], rows[:, sl, 1, :, :], xr_parts[:, t, 0, :, :],
                                            ALU.subtract).then_inc(resid_done, 1)
                    v.wait_ge(part_done, 3 * t + 2)
                    nc.vector.tensor_tensor(resid[:, 1, :, :], resid[:, 0, :, :], xr_parts[:, t, 1, :, :],
                                            ALU.subtract).then_inc(resid_done, 1)
                    v.wait_ge(part_done, 3 * t + 3)
                    v.wait_ge(resid_done, 2 * t + 2)

            @block.sync
            def _(sp):
                for t in range(NT):
                    sp.wait_ge(lin_done, 2 * t + 1)
                    sp.dma_start(xl_dram[t * P:(t + 1) * P, :],
                                 rows[:, t % 2, 0, :, :].rearrange("p a c -> p (a c)")).then_inc(stored[t % 2], 16)
                for s in range(2):
                    sp.wait_ge(stored[s], 16 * (NT // 2))


def gather_group(nc, pool, j, i, idx, idx_src, idx_ready, slot_free, ring, table, landed, begun):
    pool.wait_ge(slot_free, 2 * i + (j + 1))
    nc.gpsimd.tensor_copy(idx[:, j * KG:(j + 1) * KG], idx_src[:, bass.ds(i * (2 * KG) + j * KG, KG)]).then_inc(idx_ready, 1)
    pool.wait_ge(idx_ready, 2 * i + (j + 1))
    pool.sem_inc(begun, 1)
    for k in range(KG):
        s = j * KG + k
        nc.gpsimd.indirect_dma_start(ring[:, s, :], None, table,
                                     bass.IndirectOffsetOnAxis(ap=idx[:, s:s + 1], axis=0)).then_inc(landed[s], 16)


def edge_scores(core, srcT_i, visit_table, ident, iota_node, xl_dram, xr_parts, dloc_dram, att_row, Ev):
    nc = core.nc
    with ExitStack() as scope:
        ring = core.sb(scope, "xl_ring", [128, 2 * KG, ROW])
        idx = core.sb(scope, "idx", [128, 2 * KG], I32)
        dloc_bc = core.sb(scope, "dloc_bc", [P, 2, GE], BF16)
        onehot = core.sb(scope, "onehot_dst", [P, 2, GE], BF16)
        absz = core.sb(scope, "absz", [128, KG, D])
        prod = core.sb(scope, "prod", [128, 2, 2, D])
        red = core.sb(scope, "red", [128, KG, HEADS])
        lin = core.sb(scope, "lin", [128, KG, HEADS])
        z = [core.ps(scope, "z", [128, D]) for _ in range(KG)]
        lin_r = core.ps(scope, "lin_r", [128, 2, KG, 128])
        landed = [core.sem("row_landed") for _ in range(2 * KG)]
        slot_free, idx_ready, begun = core.sem("slot_free"), core.sem("idx_ready"), core.sem("gathers_begun")
        dloc_free = core.sem("dloc_free")
        dloc_landed = [core.sem("dloc_landed"), core.sem("dloc_landed")]
        onehot_ready, z_done, abs_done = core.sem("onehot_ready"), core.sem("z_done"), core.sem("abs_done")
        prod_done, red_done, lin_done, e_done = core.sem("prod_done"), core.sem("red_done"), core.sem("lin_done"), core.sem("e_done")
        IT = NG // 2
        with nc.Block() as block:
            @block.gpsimd
            def _(pool):
                with pool.Fori(0, IT) as i:
                    for j in range(2):
                        gather_group(nc, pool, j, i, idx, srcT_i, idx_ready, slot_free, ring, xl_dram, landed, begun)

            @block.sync
            def _(sp):
                def load(v, sl):
                    sp.dma_start(dloc_bc[:, sl, :], dloc_dram[bass.ds(v, 1), :].to_broadcast([P, GE])).then_inc(dloc_landed[sl], 16)

                sp.dma_start(dloc_bc[:, 0, :], dloc_dram[0:1, :].to_broadcast([P, GE])).then_inc(dloc_landed[0], 16)
                with sp.Fori(0, IT) as i:
                    sp.wait_ge(dloc_free, 2 * i + 1)
                    load(2 * i + 1, 1)
                    sp.wait_ge(dloc_free, 2 * i + 2)
                    load(2 * i + 2, 0)
                sp.wait_ge(dloc_landed[0], 16 * (IT + 1))
                sp.wait_ge(dloc_landed[1], 16 * IT)

            @block.tensor
            def _(pe):
                with pe.Fori(0, IT) as i:
                    for j in range(2):
                        b = pe.value_load(visit_table[0:1, 0, bass.ds(2 * i + j, 1)], min_val=0, max_val=NT - 1)
                        pe.wait_ge(onehot_ready, 2 * i + (j + 1))
                        for k in range(KG):
                            s = j * KG + k
                            pe.wait_ge(landed[s], 16 * i + 16)
                            pe.wait_ge(abs_done, 2 * KG * i + (s + 1))
                            zk = z[k][:, :].rearrange("p (a c) -> p a c", a=2)
                            nc.tensor.matmul(zk, ident[:, :], ring[:, s, :].rearrange("p (a c) -> p a c", a=2)[:, :, 0:D // 2],
                                             start=True, stop=False)
                            hot = onehot[:, j, k * 128:(k + 1) * 128]
                            for m in range(3):
                                part = xr_parts[:, bass.ds(b * 6 + 2 * m, 2), :]
                                nc.tensor.matmul(zk, hot, part[:, :, 0:D // 2], start=False, stop=(m == 2))
                            for m in range(3):
                                part = xr_parts[:, bass.ds(b * 6 + 2 * m, 2), :]
                                last = nc.tensor.matmul(lin_r[:, j, k, 0:HEADS].rearrange("p (a c) -> p a c", a=2), hot,
                                                        part[:, :, D // 2:HALF], start=(m == 0), stop=(m == 2))
                            last.then_inc(z_done, 1)

            @block.scalar
            def _(act):
                with act.Fori(0, IT) as i:
                    for j in range(2):
                        for k in range(KG):
                            s = j * KG + k
                            act.wait_ge(z_done, 2 * KG * i + (s + 1))
                            act.wait_ge(prod_done, 4 * i + 2 * j + k // 2 + 1)
                            nc.scalar.activation(absz[:, k, :], z[k][:, :], ACT.Abs).then_inc(abs_done, 1)

            @block.vector
            def _(v):
                v.sem_inc(slot_free, 2)
                v.sem_inc(dloc_free, 1)
                v.sem_inc(abs_done, KG)
                v.sem_inc(prod_done, 2)

                def hot(sl, landed_value):
                    v.wait_ge(dloc_landed[sl], landed_value)
                    nc.vector.tensor_scalar(onehot[:, sl, :], dloc_bc[:, sl, :], iota_node[0:P, :], None,
                                            ALU.is_equal).then_inc(onehot_ready, 1)

                hot(0, 16)
                v.wait_ge(onehot_ready, 1)
                v.sem_inc(dloc_free, 1)
                with v.Fori(0, IT) as i:
                    for j in range(2):
                        hot(1 - j, 16 * i + 16 * (j + 1))
                        v.wait_ge(onehot_ready, 2 * i + (j + 2))
                        v.sem_inc(dloc_free, 1)
                        for q in range(2):
                            v.wait_ge(abs_done, 2 * KG * i + (KG + j * KG + 2 * q + 2))
                            nc.vector.tensor_tensor(prod[:, q, :, :], absz[:, 2 * q:2 * q + 2, :],
                                                    att_row[:, :].unsqueeze(1).to_broadcast([128, 2, D]),
                                                    ALU.mult).then_inc(prod_done, 1)
                            v.wait_ge(prod_done, 4 * i + (2 * j + q + 3))
                            nc.vector.tensor_reduce(red[:, 2 * q:2 * q + 2, :],
                                                    prod[:, q, :, :].rearrange("p t (h c) -> p t h c", c=C),
                                                    AX.X, ALU.add).then_inc(red_done, 1)
                        rows = ring[:, j * KG:(j + 1) * KG, :].rearrange("p k (a c) -> p k a c", a=2)[:, :, :, D // 2:HALF]
                        nc.vector.tensor_tensor(lin[:, :, :].rearrange("p k (a c) -> p k a c", a=2), rows,
                                                lin_r[:, j, :, 0:HEADS].rearrange("p k (a c) -> p k a c", a=2),
                                                ALU.add).then_inc(slot_free, 1)
                        v.wait_ge(slot_free, 2 * i + (j + 3))
                        v.wait_ge(red_done, 4 * i + (2 * j + 2))
                        nc.vector.tensor_tensor(Ev[:, bass.ds(2 * KG * i + KG * j, KG), :], red[:, :, :], lin[:, :, :],
                                                ALU.add).then_inc(e_done, 1)
                        v.wait_ge(e_done, 2 * i + (j + 1))
                        v.sem_inc(begun, 1)


def segment_softmax(core, key_dram, ident, Ev):
    nc = core.nc
    with ExitStack() as scope:
        sb = lambda name, shape, dt=FP32: core.sb(scope, name, shape, dt)
        ET = sb("ET", [128, QG, 128])
        KT = sb("KT", [128, QG, 128])
        brk = sb("breaks", [128, QG * 128 + 1])
        left = sb("left", [128, QG, 128])
        right = sb("right", [128, QG, 128])
        ends = sb("ends", [128, 4, QG])
        Z = sb("Z", [HEADS, 4, QG, 16])
        pick = sb("pick", [HEADS, 16, 128])
        joined = sb("joined", [HEADS, NV])
        whole = sb("whole", [HEADS, NV])
        pass_on = sb("pass_on", [HEADS, NV])
        take = sb("take", [HEADS, NV])
        carry = sb("carry", [HEADS, 2, NV])
        cq = sb("cq", [128, 2, QG])
        tp = [core.ps(scope, "tp", [128, 4, 128]) for _ in range(2)]
        zp = [core.ps(scope, "zp", [HEADS, 5, 4, QG]) for _ in range(4)]
        cp = core.ps(scope, "cp", [128, 2, QG])
        key_landed, tp_done, evac = core.sem("key_landed"), core.sem("tp_done"), core.sem("evac")
        steps, picked, back = core.sem("steps"), core.sem("picked"), core.sem("carried_back")
        pick_ready, ends_ready, carry_ready = core.sem("pick_ready"), core.sem("ends_ready"), core.sem("carry_ready")
        shifted, exped, w_tp, w_evac = core.sem("shifted"), core.sem("exped"), core.sem("w_tp"), core.sem("w_evac")
        chunks = [(g, min(4, QG - g)) for g in range(0, QG, 4)]
        flat = lambda t: t[:, :, :].rearrange("p g e -> p (g e)")
        Ev_flat = Ev[:, :, :].rearrange("p v h -> p (v h)")
        with nc.Block() as block:
            @block.sync
            def _(sp):
                for g in range(QG):
                    tiles = key_dram[4 * g:4 * g + 4, :].rearrange("g (k e) -> (g k) e", e=128)
                    sp.dma_start(KT[:, g, :], tiles.unsqueeze(1).to_broadcast([16, HEADS, 128])).then_inc(key_landed, 16)
                sp.wait_ge(key_landed, 16 * QG)

            @block.gpsimd
            def _(pool):
                nc.gpsimd.memset(pick[:, :, :], 0.0).then_inc(pick_ready, 1)
                pool.wait_ge(pick_ready, 1)
                nc.gpsimd.affine_select(out=pick[:, :, :], in_=pick[:, :, :], compare_op=ALU.not_equal, fill=1.0, base=0,
                                        pattern=[[HEADS, 16], [-1, 128]], channel_multiplier=1).then_inc(pick_ready, 1)

            @block.tensor
            def _(pe):
                for n, (g, m) in enumerate(chunks):
                    if n >= 2:
                        pe.wait_ge(evac, n - 1)
                    for u in range(m):
                        last = nc.tensor.transpose(tp[n % 2][:, u, :], Ev_flat[:, (g + u) * 128:(g + u + 1) * 128], ident[:, :])
                    last.then_inc(tp_done, 1)
                pe.wait_ge(ends_ready, 1)
                for j in range(16):
                    last = nc.tensor.matmul(zp[j // 5][:, j % 5, :, :], ident[:, HEADS * j:HEADS * (j + 1)], ends[:, :, :],
                                            start=True, stop=True)
                last.then_inc(picked, 1)
                pe.wait_ge(carry_ready, 1)
                pe.wait_ge(pick_ready, 2)
                for j in range(16):
                    cols = carry[:, :, :].rearrange("h s (g j) -> h s g j", j=16)[:, :, :, j]
                    last = nc.tensor.matmul(cp[:, :, :], pick[:, j, :], cols, start=(j == 0), stop=(j == 15))
                last.then_inc(back, 1)
                pe.wait_ge(evac, len(chunks))
                for n, (g, m) in enumerate(chunks):
                    pe.wait_ge(exped, n + 1)
                    if n >= 2:
                        pe.wait_ge(w_evac, n - 1)
                    for u in range(m):
                        last = nc.tensor.transpose(tp[n % 2][:, u, :], ET[:, g + u, :], ident[:, :])
                    last.then_inc(w_tp, 1)

            @block.scalar
            def _(act):
                for n, (g, m) in enumerate(chunks):
                    act.wait_ge(tp_done, n + 1)
                    nc.scalar.activation(ET[:, g:g + m, :], tp[n % 2][:, 0:m, :], ACT.Copy).then_inc(evac, 1)
                for n, (g, m) in enumerate(chunks):
                    act.wait_ge(shifted, n + 1)
                    nc.scalar.activation(ET[:, g:g + m, :], right[:, g:g + m, :], ACT.Exp).then_inc(exped, 1)
                for n, (g, m) in enumerate(chunks):
                    act.wait_ge(w_tp, n + 1)
                    nc.scalar.activation(Ev_flat[:, g * 128:(g + m) * 128].rearrange("p (u e) -> p u e", e=128),
                                         tp[n % 2][:, 0:m, :], ACT.Copy).then_inc(w_evac, 1)

            @block.vector
            def _(v):
                link = linker(v, steps)
                b3 = brk[:, 0:QG * 128].rearrange("p (g e) -> p g e", e=128)
                link(nc.vector.memset(b3[:, :, 0:1], -BIG))
                link(nc.vector.memset(brk[:, QG * 128:QG * 128 + 1], -BIG))
                v.wait_ge(key_landed, 16 * QG)
                link(nc.vector.tensor_tensor(b3[:, :, 1:128], KT[:, :, 1:128], KT[:, :, 0:127], ALU.is_equal))
                link(nc.vector.tensor_scalar(b3[:, :, 1:128], b3[:, :, 1:128], -1.0, BIG, ALU.add, ALU.mult))
                v.wait_ge(evac, len(chunks))
                link(nc.vector.tensor_tensor_scan(flat(left), brk[:, 0:QG * 128], flat(ET), -BIG, ALU.add, ALU.max))
                link(nc.vector.tensor_tensor_scan(flat(right)[:, ::-1], brk[:, 1:QG * 128 + 1][:, ::-1], flat(ET)[:, ::-1],
                                                  -BIG, ALU.add, ALU.max))
                link(nc.vector.tensor_copy(ends[:, 0, :], KT[:, :, 0]))
                link(nc.vector.tensor_copy(ends[:, 1, :], KT[:, :, 127]))
                link(nc.vector.tensor_copy(ends[:, 2, :], left[:, :, 127]))
                nc.vector.tensor_copy(ends[:, 3, :], right[:, :, 0]).then_inc(ends_ready, 1)
                link(nc.vector.tensor_tensor(flat(left), flat(left), flat(right), ALU.max))
                v.wait_ge(picked, 1)
                for n in range(4):
                    m = min(5, 16 - 5 * n)
                    link(nc.vector.tensor_copy(Z[:, :, :, 5 * n:5 * n + m], zp[n][:, 0:m, :, :].rearrange("h j a g -> h a g j")))
                z = Z[:, :, :, :].rearrange("h a g j -> h a (g j)")
                k0, k1, lmax, fmax = (z[:, a, :] for a in range(4))
                last = NV - 1
                link(nc.vector.tensor_tensor(joined[:, 1:NV], k0[:, 1:NV], k1[:, 0:last], ALU.is_equal))
                link(nc.vector.tensor_tensor(whole[:, :], k0, k1, ALU.is_equal))
                link(nc.vector.memset(carry[:, :, :], -BIG))
                link(nc.vector.tensor_tensor(pass_on[:, 1:NV], joined[:, 1:NV], whole[:, 0:last], ALU.mult))
                link(nc.vector.tensor_scalar(pass_on[:, 1:NV], pass_on[:, 1:NV], -1.0, BIG, ALU.add, ALU.mult))
                link(nc.vector.tensor_scalar(joined[:, 1:NV], joined[:, 1:NV], -1.0, BIG, ALU.add, ALU.mult))
                link(nc.vector.tensor_tensor(take[:, 1:NV], joined[:, 1:NV], lmax[:, 0:last], ALU.add))
                link(nc.vector.tensor_tensor_scan(carry[:, 0, 1:NV], pass_on[:, 1:NV], take[:, 1:NV], -BIG, ALU.add, ALU.max))
                link(nc.vector.tensor_scalar(whole[:, :], whole[:, :], -1.0, BIG, ALU.add, ALU.mult))
                link(nc.vector.tensor_tensor(pass_on[:, 1:NV], joined[:, 1:NV], whole[:, 1:NV], ALU.add))
                link(nc.vector.tensor_tensor(take[:, 1:NV], joined[:, 1:NV], fmax[:, 1:NV], ALU.add))
                nc.vector.tensor_tensor_scan(carry[:, 1, 0:last][:, ::-1], pass_on[:, 1:NV][:, ::-1], take[:, 1:NV][:, ::-1],
                                             -BIG, ALU.add, ALU.max).then_inc(carry_ready, 1)
                v.wait_ge(back, 1)
                link(nc.vector.tensor_copy(cq[:, :, :], cp[:, :, :]))
                for side, edge in ((0, 0), (1, 127)):
                    link(nc.vector.tensor_tensor(right[:, :, :], KT[:, :, :],
                                                 KT[:, :, edge:edge + 1].to_broadcast([128, QG, 128]), ALU.is_equal))
                    link(nc.vector.tensor_scalar(flat(right), flat(right), -1.0, BIG, ALU.add, ALU.mult))
                    link(nc.vector.tensor_tensor(right[:, :, :], right[:, :, :],
                                                 cq[:, side, :].unsqueeze(2).to_broadcast([128, QG, 128]), ALU.add))
                    link(nc.vector.tensor_tensor(flat(left), flat(left), flat(right), ALU.max))
                for n, (g, m) in enumerate(chunks):
                    nc.vector.tensor_tensor(right[:, g:g + m, :], ET[:, g:g + m, :], left[:, g:g + m, :],
                                            ALU.subtract).then_inc(shifted, 1)


def aggregate(core, srcT_i, srcT_f, dlT, visit_table, iota_row, iota_row16, xl_dram, Wv, gat_bias, X, X2, AT):
    nc = core.nc
    with ExitStack() as scope:
        ring = core.sb(scope, "xl_ring", [128, 2 * KG, ROW])
        idx = core.sb(scope, "idx", [128, 2 * KG], I32)
        hot = core.sb(scope, "hot", [128, 2, KG, P])
        hot_b = core.sb(scope, "hot_b", [128, 2, KG, P], BF16)
        hot_src = core.sb(scope, "hot_src", [128, 2, N], BF16)
        msg = core.sb(scope, "msg", [128, 2 * KG, 2, HALF])
        zero = core.sb(scope, "zero", [128, 512], BF16)
        rden = core.sb(scope, "rden", [P, 2, HEADS // 2])
        gat = core.sb(scope, "gat", [P, D])
        sums = core.ps(scope, "sums", [P, 2, 512])
        cnt = core.ps(scope, "cnt", [P, 3, 512])
        landed = [core.sem("row_landed") for _ in range(2 * KG)]
        slot_free, idx_ready, begun = core.sem("slot_free"), core.sem("idx_ready"), core.sem("gathers_begun")
        hot_ready, hotb_ready, hsrc_ready = core.sem("hot_ready"), core.sem("hotb_ready"), core.sem("hot_src_ready")
        w_copied, msg_ready = core.sem("w_copied"), core.sem("msg_ready")
        mm_done, group_done = core.sem("mm_done"), core.sem("group_done")
        sums_read, cnt_read, zeroed = core.sem("sums_read"), core.sem("cnt_read"), core.sem("zeroed")
        cnt_evac, steps = core.sem("cnt_evac"), core.sem("steps")
        IT = NG // 2
        PER = [4, 4, 2]
        with nc.Block() as block:
            @block.gpsimd
            def _(pool):
                with pool.Fori(0, IT) as i:
                    for j in range(2):
                        gather_group(nc, pool, j, i, idx, srcT_i, idx_ready, slot_free, ring, xl_dram, landed, begun)

            @block.tensor
            def _(pe):
                pe.wait_ge(zeroed, 1)
                with pe.Fori(0, IT) as i:
                    for j in range(2):
                        first = pe.value_load(visit_table[0:1, 1, bass.ds(2 * i + j, 1)], min_val=0, max_val=1)
                        b = pe.value_load(visit_table[0:1, 0, bass.ds(2 * i + j, 1)], min_val=0, max_val=NT - 1)
                        with pe.If(first > 0):
                            pe.wait_ge(sums_read, b + 1)
                            pe.wait_ge(cnt_read, b + 1)
                            for bank in (sums[:, 0, :], sums[:, 1, :], cnt[:, 0, :], cnt[:, 1, :], cnt[:, 2, :]):
                                nc.tensor.matmul(bank, zero[:, 0:P], zero[:, :], start=True, stop=True)
                        pe.wait_ge(hotb_ready, 2 * i + (j + 1))
                        for k in range(KG):
                            s = j * KG + k
                            pe.wait_ge(msg_ready, 2 * KG * i + (s + 1))
                            for a in range(2):
                                nc.tensor.matmul(sums[:, a, 0:HALF], hot[:, j, k, :], msg[:, s, a, :],
                                                 start=False, stop=True, skip_group_check=True)
                            pe.wait_ge(hsrc_ready, 2 * KG * i + (s + 1))
                            for t in range(NT):
                                last = nc.tensor.matmul(cnt[:, t // 4, (t % 4) * P:(t % 4 + 1) * P],
                                                        hot_src[:, k % 2, t * P:(t + 1) * P], hot_b[:, j, k, :],
                                                        start=False, stop=True, skip_group_check=True)
                            last.then_inc(mm_done, 1)

            @block.scalar
            def _(act):
                with act.Fori(0, IT) as i:
                    for j in range(2):
                        act.wait_ge(mm_done, 2 * KG * i + KG * (j + 1))
                        act.wait_ge(hot_ready, 2 * i + (j + 1))
                        nc.scalar.activation(hot_b[:, j, :, :], hot[:, j, :, :], ACT.Copy).then_inc(hotb_ready, 1)
                        w = Wv[:, bass.ds(2 * KG * i + KG * j, KG), :].rearrange("p k (a h) -> p k a h", a=2)
                        nc.scalar.activation(msg[:, j * KG:(j + 1) * KG, :, D // 2:HALF], w, ACT.Copy).then_inc(w_copied, 1)
                        last = act.value_load(visit_table[0:1, 2, bass.ds(2 * i + j, 1)], min_val=0, max_val=1)
                        b = act.value_load(visit_table[0:1, 0, bass.ds(2 * i + j, 1)], min_val=0, max_val=NT - 1)
                        with act.If(last > 0):
                            act.wait_ge(mm_done, 2 * KG * i + KG * (j + 3))
                            for q in range(3):
                                nc.scalar.activation(AT[:, 4 * q:4 * q + PER[q], bass.ds(b * P, P)],
                                                     cnt[:, q, 0:PER[q] * P].rearrange("p (t n) -> p t n", n=P),
                                                     ACT.Copy).then_inc(cnt_evac, 1)
                            act.wait_ge(cnt_evac, 3 * b + 3)
                            act.sem_inc(cnt_read, 1)
                        act.sem_inc(steps, 1)

            @block.vector
            def _(v):
                v.sem_inc(slot_free, 2)
                v.sem_inc(sums_read, 1)
                v.sem_inc(cnt_read, 1)
                v.sem_inc(mm_done, 2 * KG)
                nc.vector.memset(zero[:, :], 0.0).then_inc(zeroed, 1)
                den = core.sem("den_steps")
                with v.Fori(0, IT) as i:
                    for j in range(2):
                        v.wait_ge(mm_done, 2 * KG * i + KG * (j + 1))
                        nc.vector.tensor_tensor(hot[:, j, :, :], iota_row[:, :].unsqueeze(1).to_broadcast([128, KG, P]),
                                                dlT[:, bass.ds(2 * KG * i + KG * j, KG)].unsqueeze(2).to_broadcast([128, KG, P]),
                                                ALU.is_equal).then_inc(hot_ready, 1)
                        for k in range(KG):
                            s = j * KG + k
                            v.wait_ge(mm_done, 2 * KG * i + (2 * KG + s - 1))
                            nc.vector.tensor_scalar(hot_src[:, k % 2, :], iota_row16[:, :],
                                                    srcT_f[:, bass.ds(2 * KG * i + s, 1)], None,
                                                    ALU.is_equal).then_inc(hsrc_ready, 1)
                            if k == 0:
                                v.wait_ge(w_copied, 2 * i + (j + 1))
                            v.wait_ge(landed[s], 16 * i + 16)
                            w = Wv[:, bass.ds(2 * KG * i + s, 1), :].rearrange("p u (a h) -> p (u a) h", a=2)
                            nc.vector.tensor_tensor(
                                msg[:, s, :, 0:D // 2].rearrange("p a (h c) -> p a h c", c=C),
                                ring[:, s, :].rearrange("p (a c) -> p a c", a=2)[:, :, 0:D // 2].rearrange("p a (h c) -> p a h c", c=C),
                                w.unsqueeze(3).to_broadcast([128, 2, HEADS // 2, C]), ALU.mult).then_inc(msg_ready, 1)
                        v.wait_ge(msg_ready, 2 * KG * i + KG * (j + 1))
                        v.sem_inc(slot_free, 1)
                        last = v.value_load(visit_table[0:1, 2, bass.ds(2 * i + j, 1)], min_val=0, max_val=1)
                        b = v.value_load(visit_table[0:1, 0, bass.ds(2 * i + j, 1)], min_val=0, max_val=NT - 1)
                        with v.If(last > 0):
                            v.wait_ge(mm_done, 2 * KG * i + KG * (j + 3))
                            nc.vector.tensor_scalar(rden[:, :, :], sums[:, :, D // 2:HALF], 1e-16, None, ALU.add).then_inc(den, 1)
                            v.wait_ge(den, 5 * b + 1)
                            nc.vector.reciprocal(rden[:, :, :], rden[:, :, :]).then_inc(den, 1)
                            v.wait_ge(den, 5 * b + 2)
                            nc.vector.tensor_tensor(gat[:, :].rearrange("p (a h c) -> p a h c", a=2, c=C),
                                                    sums[:, :, 0:D // 2].rearrange("p a (h c) -> p a h c", c=C),
                                                    rden[:, :, :].unsqueeze(3).to_broadcast([P, 2, HEADS // 2, C]),
                                                    ALU.mult).then_inc(den, 1)
                            v.wait_ge(den, 5 * b + 3)
                            v.sem_inc(sums_read, 1)
                            nc.vector.tensor_tensor(gat[:, :], gat[:, :], gat_bias[0:P, :], ALU.add).then_inc(den, 1)
                            v.wait_ge(den, 5 * b + 4)
                            nc.vector.tensor_tensor(X2[:, bass.ds(b * D, D)], gat[:, :], X[:, bass.ds(b * D, D)],
                                                    ALU.add).then_inc(den, 1)
                            v.wait_ge(den, 5 * b + 5)
                            v.sem_inc(steps, 1)
                        v.sem_inc(steps, 1)


def ffn(core, hT, W1, b1, W2, b2_row, X, X2):
    nc = core.nc
    NB = 2 * P
    BL = N // NB
    FK = FF // 128
    with ExitStack() as scope:
        gT = core.sb(scope, "gT", [128, FK, NB])
        up = [core.ps(scope, "up", [128, NB]) for _ in range(4)]
        down = [core.ps(scope, "down", [P, D]) for _ in range(2)]
        up_done, gelu_done, down_done, added, pre = (core.sem(n) for n in ("up_done", "gelu_done", "down_done", "added", "pre"))
        with nc.Block() as block:
            @block.tensor
            def _(pe):
                for nb in range(BL):
                    for f in range(FK):
                        n = nb * FK + f
                        if n >= 4:
                            pe.wait_ge(gelu_done, n - 3)
                        for k in range(CK):
                            last = nc.tensor.matmul(up[n % 4][:, :], W1[:, k, f * 128:(f + 1) * 128],
                                                    hT[:, k, nb * NB:(nb + 1) * NB], start=(k == 0), stop=(k == CK - 1))
                        last.then_inc(up_done, 1)
                    for u in range(2):
                        t = 2 * nb + u
                        if t >= 2:
                            pe.wait_ge(added, t - 1)
                        for f in range(FK):
                            pe.wait_ge(gelu_done, nb * FK + f + 1)
                            last = nc.tensor.matmul(down[u][:, :], gT[:, f, u * P:(u + 1) * P], W2[:, f, :],
                                                    start=(f == 0), stop=(f == FK - 1))
                        last.then_inc(down_done, 1)

            @block.scalar
            def _(act):
                for nb in range(BL):
                    if nb >= 1:
                        act.wait_ge(down_done, 2 * nb)
                    for f in range(FK):
                        n = nb * FK + f
                        act.wait_ge(up_done, n + 1)
                        nc.scalar.activation(gT[:, f, :], up[n % 4][:, :], ACT.Gelu, bias=b1[:, f:f + 1]).then_inc(gelu_done, 1)

            @block.vector
            def _(v):
                for t in range(NT):
                    nc.vector.tensor_tensor(X[:, t, :], X[:, t, :], X2[:, t, :], ALU.add).then_inc(pre, 1)
                for t in range(NT):
                    v.wait_ge(pre, t + 1)
                    nc.vector.tensor_tensor(X[:, t, :], X[:, t, :], b2_row[0:P, :], ALU.add).then_inc(pre, 1)
                for t in range(NT):
                    v.wait_ge(down_done, t + 1)
                    v.wait_ge(pre, NT + t + 1)
                    nc.vector.tensor_tensor(X[:, t, :], X[:, t, :], down[t % 2][:, :], ALU.add).then_inc(added, 1)


def sage_layer(core, XT, AT, Wp, bp_row, Wl, bl_row, Wr, H, GT, inv_row, Y, residual=None):
    nc = core.nc
    groups = [(0, 3), (3, 3), (6, 4)]
    with ExitStack() as scope:
        tmp = core.sb(scope, "tmp", [P, 2, D])
        acc = [core.ps(scope, "acc", [P, D]) for _ in range(3)]
        agg = [core.ps(scope, "agg", [128, D]) for _ in range(3)]
        h_mm, h_add, h_relu = core.sem("h_product"), core.sem("h_biased"), core.sem("h_ready")
        a_mm, a_done, o_mm, o_add, o_done = (core.sem(n) for n in ("agg_product", "agg_ready", "out_product", "out_biased", "out_ready"))
        with nc.Block() as block:
            @block.tensor
            def _(pe):
                for t in range(NT):
                    if t >= 3:
                        pe.wait_ge(h_add, t - 2)
                    for k in range(CK):
                        last = nc.tensor.matmul(acc[t % 3][:, :], XT[:, k, t * P:(t + 1) * P], Wp[:, k, :],
                                                start=(k == 0), stop=(k == CK - 1))
                    last.then_inc(h_mm, 1)
                n = 0
                for c in range(CK):
                    for g0, gn in groups:
                        if n >= 3:
                            pe.wait_ge(a_done, n - 2)
                        for s in range(NT):
                            if n == 0:
                                pe.wait_ge(h_relu, s + 1)
                            last = nc.tensor.matmul(agg[n % 3][:, 0:gn * P], H[:, s, c * 128:(c + 1) * 128],
                                                    AT[:, s, g0 * P:(g0 + gn) * P], start=(s == 0), stop=(s == NT - 1))
                        last.then_inc(a_mm, 1)
                        n += 1
                pe.wait_ge(h_add, NT)
                for t in range(NT):
                    if t >= 3:
                        pe.wait_ge(o_add, t - 2)
                    for k in range(CK):
                        nc.tensor.matmul(acc[t % 3][:, :], XT[:, k, t * P:(t + 1) * P], Wr[:, k, :], start=(k == 0), stop=False)
                    pe.wait_ge(a_done, n)
                    for k in range(CK):
                        last = nc.tensor.matmul(acc[t % 3][:, :], GT[:, k, t * P:(t + 1) * P], Wl[:, k, :],
                                                start=False, stop=(k == CK - 1))
                    last.then_inc(o_mm, 1)

            @block.vector
            def _(v):
                for t in range(NT):
                    v.wait_ge(h_mm, t + 1)
                    if t >= 2:
                        v.wait_ge(h_relu, t - 1)
                    nc.vector.tensor_tensor(tmp[:, t % 2, :], acc[t % 3][:, :], bp_row[0:P, :], ALU.add).then_inc(h_add, 1)
                n = 0
                for c in range(CK):
                    for g0, gn in groups:
                        v.wait_ge(a_mm, n + 1)
                        nc.vector.tensor_tensor(GT[:, c, g0 * P:(g0 + gn) * P], agg[n % 3][:, 0:gn * P],
                                                inv_row[:, g0 * P:(g0 + gn) * P], ALU.mult).then_inc(a_done, 1)
                        n += 1
                v.wait_ge(h_relu, NT)
                for t in range(NT):
                    v.wait_ge(o_mm, t + 1)
                    if residual is None:
                        if t >= 2:
                            v.wait_ge(o_done, t - 1)
                        nc.vector.tensor_tensor(tmp[:, t % 2, :], acc[t % 3][:, :], bl_row[0:P, :], ALU.add).then_inc(o_add, 1)
                    else:
                        if t >= 2:
                            v.wait_ge(o_done, t - 1)
                        nc.vector.tensor_tensor(tmp[:, t % 2, :], acc[t % 3][:, :], bl_row[0:P, :], ALU.add).then_inc(o_add, 1)
                        v.wait_ge(o_add, t + 1)
                        nc.vector.tensor_tensor(Y[:, t, :], residual[:, t, :], tmp[:, t % 2, :], ALU.add).then_inc(o_done, 1)

            @block.scalar
            def _(act):
                for t in range(NT):
                    act.wait_ge(h_add, t + 1)
                    nc.scalar.activation(H[:, t, :], tmp[:, t % 2, :], ACT.Relu).then_inc(h_relu, 1)
                if residual is None:
                    for t in range(NT):
                        act.wait_ge(o_add, t + 1)
                        nc.scalar.activation(Y[:, t, :], tmp[:, t % 2, :], ACT.Relu).then_inc(o_done, 1)


def counts_block(core, AT, inv_row):
    nc = core.nc
    with ExitStack() as scope:
        ones = core.sb(scope, "ones", [P, 128])
        most = core.sb(scope, "most", [128, N])
        cnt = [core.ps(scope, "cnt", [128, 500]) for _ in range(3)]
        ready, summed, steps = core.sem("ones_ready"), core.sem("summed"), core.sem("steps")
        cols = [(0, 500), (500, 500), (1000, 250)]
        with nc.Block() as block:
            @block.tensor
            def _(pe):
                pe.wait_ge(ready, 1)
                for n, (c0, cn) in enumerate(cols):
                    for s in range(NT):
                        last = nc.tensor.matmul(cnt[n][:, 0:cn], ones[:, :], AT[:, s, c0:c0 + cn], start=(s == 0), stop=(s == NT - 1))
                last.then_inc(summed, 1)

            @block.vector
            def _(v):
                nc.vector.memset(ones[:, :], 1.0).then_inc(ready, 1)
                link = linker(v, steps)
                v.wait_ge(summed, 1)
                for n, (c0, cn) in enumerate(cols):
                    link(nc.vector.tensor_scalar(most[:, c0:c0 + cn], cnt[n][:, 0:cn], 1.0, None, ALU.max))
                link(nc.vector.reciprocal(inv_row[:, :], most[:, :]))


def scale_rows(core, att_raw, att_row, lin_row):
    nc = core.nc
    sem = core.sem("scaled")
    with nc.Block() as block:
        @block.vector
        def _(v):
            link = linker(v, sem)
            link(nc.vector.tensor_scalar(att_row[:, :], att_raw[:, :], 0.4, None, ALU.mult))
            link(nc.vector.tensor_scalar(lin_row[:, :], att_raw[0:P, :], 0.6, None, ALU.mult))


def gnn_kernel(nc, x, src, dst, ln1_g, ln1_b, Wl, Wr, att, gat_bias, ln2_g, ln2_b, W1, b1, W2, b2, sage, norms, out):
    ctx = ExitStack()
    with ctx:
        core = Core(nc, ctx)
        edges_dram = nc.dram_tensor("edge_groups", (EGP, 2 * GE), I32).ap()
        dloc_dram = nc.dram_tensor("visit_dloc", (NGP, GE), BF16).ap()
        key_dram = nc.dram_tensor("visit_keys", (NGP, GE), FP32).ap()
        xl_dram = nc.dram_tensor("xl_rows", (N, ROW), FP32).ap()
        wide = lambda v, rows=128: row_view(v).to_broadcast([rows, D])
        kpn = lambda w: w.rearrange("(k p) n -> p k n", p=128)
        chan = lambda v: v.rearrange("(k p) -> p k", p=128)

        ident = core.sb(ctx, "ident", [128, 128])
        iota_node = core.sb(ctx, "iota_node", [128, 1])
        iota_row = core.sb(ctx, "iota_row", [128, P])
        X = core.sb(ctx, "X", [P, NT * D])
        X3 = X[:, :].rearrange("p (t c) -> p t c", c=D)
        small = core.sb(ctx, "small", [128, 32])
        AT = core.sb(ctx, "AT", [P, NT, N])
        X2 = core.sb(ctx, "X2", [P, NT * D])
        with ExitStack() as edge:
            iota_row16 = core.sb(edge, "iota_row16", [128, N], I16)
            visit_table = core.sb(edge, "visit_table", [1, 3, NG], I32)
            srcT_i = core.sb(edge, "srcT_i", [128, NV], I32)
            srcT_f = core.sb(edge, "srcT_f", [128, NV])
            dlT = core.sb(edge, "dlT", [128, NV])
            Ev = core.sb(edge, "Ev", [128, NV, HEADS])
            gb_row = core.sb(edge, "gat_bias", [128, D])
            setup_constants(core, ident, iota_node, iota_row, iota_row16)
            dst_f = core.sb(edge, "dst_f", [EGP, GE])
            order_edges(core, src, dst, ident, dst_f, edges_dram)
            plan_visits(core, dst_f, ident, srcT_i, srcT_f, dlT, visit_table, edges_dram, dloc_dram, key_dram)
            with ExitStack() as first:
                att_raw = core.sb(first, "att_raw", [128, D])
                att_row = core.sb(first, "att_row", [128, D])
                lin_row = core.sb(first, "lin_row", [P, D])
                xr_parts = core.sb(first, "xr_parts", [P, NT * 3 * 2, HALF], BF16)
                with ExitStack() as dense:
                    hT = core.sb(dense, "hT", [128, CK, N])
                    wl = core.sb(dense, "wl", [128, CK, D])
                    wr = core.sb(dense, "wr", [128, CK, D])
                    with nc.allow_non_contiguous_dma(reason="small vectors laid along partitions"):
                        load_block(core, [
                            (X3, x.rearrange("(t p) c -> p t c", p=P)), (wl[:, :, :], kpn(Wl)), (wr[:, :, :], kpn(Wr)),
                            (att_raw[:, :], wide(att)), (gb_row[:, :], wide(gat_bias)),
                            (small[:, 0:4], chan(ln1_g)), (small[:, 4:8], chan(ln1_b))])
                    scale_rows(core, att_raw, att_row, lin_row)
                    norm_block(core, X3, hT, ident, small[:, 0:4], small[:, 4:8])
                    build_tables(core, hT, wl, wr, att_row, lin_row, xl_dram,
                                 xr_parts[:, :, :].rearrange("p (t m a) c -> p t m a c", m=3, a=2))
                edge_scores(core, srcT_i, visit_table, ident, iota_node, xl_dram, xr_parts, dloc_dram, att_row, Ev)
            segment_softmax(core, key_dram, ident, Ev)
            aggregate(core, srcT_i, srcT_f, dlT, visit_table, iota_row, iota_row16, xl_dram, Ev, gb_row, X, X2, AT)
        core.recycle()
        X23 = X2[:, :].rearrange("p (t c) -> p t c", c=D)

        XT = core.sb(ctx, "XT", [128, CK, N])
        with ExitStack() as mlp:
            w1 = core.sb(mlp, "w1", [128, CK, FF])
            w2 = core.sb(mlp, "w2", [128, FF // 128, D])
            b2_row = core.sb(mlp, "b2", [128, D])
            with nc.allow_non_contiguous_dma(reason="small vectors laid along partitions"):
                load_block(core, [(w1[:, :, :], kpn(W1)), (w2[:, :, :], kpn(W2)), (b2_row[:, :], wide(b2)),
                                  (small[:, 0:4], chan(ln2_g)), (small[:, 4:8], chan(ln2_b)), (small[:, 8:24], chan(b1))])
            norm_block(core, X23, XT, ident, small[:, 0:4], small[:, 4:8])
            ffn(core, XT, w1, small[:, 8:24], w2, b2_row, X3, X23)
        H = core.sb(ctx, "H", [P, NT, D])
        GT = core.sb(ctx, "GT", [128, CK, N])
        inv_row = core.sb(ctx, "inv_row", [128, N])
        wp, wl2, wr2 = (core.sb(ctx, n, [128, CK, D]) for n in ("wp", "wl", "wr"))
        bp_row, bl_row = (core.sb(ctx, n, [128, D]) for n in ("bp_row", "bl_row"))
        norm_block(core, X3, XT, ident, normed=X23)
        counts_block(core, AT, inv_row)
        for l in range(3):
            core.recycle()
            Wp_, bp_, Wl_, bl_, Wr_ = sage[l]
            pairs = [(wp[:, :, :], kpn(Wp_)), (wl2[:, :, :], kpn(Wl_)), (wr2[:, :, :], kpn(Wr_)),
                     (bp_row[:, :], wide(bp_)), (bl_row[:, :], wide(bl_))]
            if l < 2:
                pairs += [(small[:, 0:4], chan(norms[l][0])), (small[:, 4:8], chan(norms[l][1]))]
            with nc.allow_non_contiguous_dma(reason="small vectors laid along partitions"):
                load_block(core, pairs)
            sage_layer(core, XT, AT, wp, bp_row, wl2, bl_row, wr2, H, GT, inv_row, X3, residual=X23 if l == 2 else None)
            if l < 2:
                norm_block(core, X3, XT, ident, small[:, 0:4], small[:, 4:8])
        norm_block(core, X3, None, ident, normed=H, out=out)


_TRANSPOSED = [f'L1_gnn_{w}{l}' for l in range(3) for w in ('Wp', 'Wl', 'Wr')]
_INS = ['x', 'src', 'dst', 'L0_gnn_ln1_g', 'L0_gnn_ln1_b', 'L0_gnn_Wl', 'L0_gnn_Wr', 'L0_gnn_att', 'L0_gnn_gat_bias',
        'L0_gnn_ln2_g', 'L0_gnn_ln2_b', 'L0_gnn_W1', 'L0_gnn_b1', 'L0_gnn_W2', 'L0_gnn_b2']
_SAGE = [[f'L1_gnn_{w}{l}' for w in ('Wp', 'bp', 'Wl', 'bl', 'Wr')] for l in range(3)]
_NORMS = [[f'L1_gnn_{w}{l}' for w in ('g', 'be')] for l in range(2)]


def kernel(**inputs):
    import numpy as _np
    import concourse.bacc as _bacc
    from concourse import mybir as _mybir
    from concourse.bass_utils import run_bass_kernel_spmd as _run

    nc = _bacc.Bacc("TRN2", target_bir_lowering=False, num_devices=1)
    arrays = {}

    def given(name):
        a = _np.asarray(inputs[name])
        if name in _TRANSPOSED:
            a = a.T
        if name == 'L0_gnn_att':
            a = a.reshape(-1)
        a = _np.ascontiguousarray(a)
        arrays[f"in_{name}"] = a
        return nc.dram_tensor(f"in_{name}", a.shape, _mybir.dt.from_np(a.dtype), kind="ExternalInput").ap()

    args = [given(n) for n in _INS]
    sage = [[given(n) for n in layer] for layer in _SAGE]
    norms = [[given(n) for n in layer] for layer in _NORMS]
    out = nc.dram_tensor("out_0", (N, D), _mybir.dt.float32, kind="ExternalOutput").ap()
    gnn_kernel(nc, *args, sage, norms, out)
    r = _run(nc, [arrays], core_ids=[0])
    return r.results[0]["out_0"]
```
